# Optimizing a Trainium2 kernel written in Bass

```python
import numpy as np
import jax
import jax.numpy as jnp

def _softmax(x, axis=-1):
    return jax.nn.softmax(x, axis=axis)

def _gelu(x):
    return jax.nn.gelu(x, approximate=True)

def _silu(x):
    return jax.nn.silu(x)

def _sigmoid(x):
    return jax.nn.sigmoid(x)

def _layernorm(x, axis=-1, eps=1e-05):
    m = jnp.mean(x, axis=axis, keepdims=True)
    v = jnp.var(x, axis=axis, keepdims=True)
    return (x - m) / jnp.sqrt(v + eps)

def _scatter_add(tgt, idx, src, axis=0):
    return tgt.at[idx].add(src)

def _segment_sum(src, seg, n):
    return jax.ops.segment_sum(src, seg, n)
kernel_name = 'mk_gnn_preln_d2_gnn_r8_b9e438'

def setup_inputs(seed: int=0):
    np.random.seed(seed)
    _w = jnp.asarray

    def _rec_inputs():
        import jax
        import jax.numpy as jnp
        _gk = jax.random.key(seed)
        x = -0.000202 + 1 * jax.random.normal(jax.random.fold_in(_gk, 1), (6250, 128), jnp.float32)
        src = jax.random.randint(jax.random.fold_in(_gk, 2), (200000,), 0, 6250, jnp.int32)
        dst = jax.random.randint(jax.random.fold_in(_gk, 3), (200000,), 0, 6250, jnp.int32)
        _o = jnp.argsort(dst, stable=True)
        src = src[_o]
        dst = dst[_o]
        edge_attr_64 = 0.000167468 + 1.0002 * jax.random.normal(jax.random.fold_in(_gk, 11), (200000, 64), jnp.float32)
        return (x, src, dst, edge_attr_64)
    x, src, dst, edge_attr_64 = _rec_inputs()

    def _L0_gnn_setup():
        import jax, jax.numpy as jnp
        import numpy as np
        N_NODES = 6250
        N_EDGES = 100000
        IN_CH = 128
        HEADS = 4
        OUT_CH = 32
        key = jax.random.key(seed)
        k1, k2, k3, k4, k5 = jax.random.split(key, 5)
        x = jax.random.normal(k1, (N_NODES, IN_CH), dtype=jnp.float32)
        edge_index = jax.random.randint(k2, (2, N_EDGES), 0, N_NODES, dtype=jnp.int64)
        W = jax.random.normal(k3, (IN_CH, HEADS * OUT_CH), dtype=jnp.float32) * 0.1
        att = jax.random.normal(k4, (1, HEADS, 2 * OUT_CH), dtype=jnp.float32) * 0.1
        bias = jax.random.normal(k5, (HEADS * OUT_CH,), dtype=jnp.float32) * 0.01
        return {'x': x, 'edge_index': edge_index, 'W': W, 'att': att, 'bias': bias}
    _L0_gnn_all = _L0_gnn_setup()
    _L0_gnn_in = {k: v for k, v in _L0_gnn_all.items() if k in ('W', 'att', 'bias')}
    del _L0_gnn_all

    def _L1_gnn_setup():
        import jax, jax.numpy as jnp
        import numpy as np
        N_NODES = 12500
        NODE_DIM = 128
        EDGE_DIM = 64
        HIDDEN_DIM = 256
        N_EDGES = 80000
        key = jax.random.key(seed)
        k1, k2, k3, k4, k5, k6, k7 = jax.random.split(key, 7)
        x = jax.random.normal(k1, (N_NODES, NODE_DIM), dtype=jnp.float32)
        edge_index = jax.random.randint(k2, (2, N_EDGES), 0, N_NODES, dtype=jnp.int64)
        edge_attr = jax.random.normal(k3, (N_EDGES, EDGE_DIM), dtype=jnp.float32)
        in_dim = 2 * NODE_DIM + EDGE_DIM
        lim1 = 1.0 / np.sqrt(in_dim)
        lim2 = 1.0 / np.sqrt(HIDDEN_DIM)
        W1 = jax.random.uniform(k4, (in_dim, HIDDEN_DIM), minval=-lim1, maxval=lim1, dtype=jnp.float32)
        b1 = jax.random.uniform(k5, (HIDDEN_DIM,), minval=-lim1, maxval=lim1, dtype=jnp.float32)
        W2 = jax.random.uniform(k6, (HIDDEN_DIM, NODE_DIM), minval=-lim2, maxval=lim2, dtype=jnp.float32)
        b2 = jax.random.uniform(k7, (NODE_DIM,), minval=-lim2, maxval=lim2, dtype=jnp.float32)
        return {'x': x, 'edge_index': edge_index, 'edge_attr': edge_attr, 'W1': W1, 'b1': b1, 'W2': W2, 'b2': b2}
    _L1_gnn_all = _L1_gnn_setup()
    _L1_gnn_in = {k: v for k, v in _L1_gnn_all.items() if k in ('W1', 'b1', 'W2', 'b2')}
    del _L1_gnn_all
    return {'x': x, 'src': src, 'dst': dst, 'edge_attr_64': edge_attr_64, 'L0_gnn_W': _L0_gnn_in['W'], 'L0_gnn_att': _L0_gnn_in['att'], 'L0_gnn_bias': _L0_gnn_in['bias'], 'L1_gnn_W1': _L1_gnn_in['W1'], 'L1_gnn_b1': _L1_gnn_in['b1'], 'L1_gnn_W2': _L1_gnn_in['W2'], 'L1_gnn_b2': _L1_gnn_in['b2']}

def reference(x, src, dst, edge_attr_64, L0_gnn_W, L0_gnn_att, L0_gnn_bias, L1_gnn_W1, L1_gnn_b1, L1_gnn_W2, L1_gnn_b2):
    import jax
    import jax.numpy as jnp

    def _L0_gnn_ref(x, edge_index, W, att, bias):
        import jax, jax.numpy as jnp
        import numpy as np
        N_NODES = 6250
        N_EDGES = 100000
        IN_CH = 128
        HEADS = 4
        OUT_CH = 32
        N = x.shape[0]
        E = edge_index.shape[1]
        H, C = (HEADS, OUT_CH)
        h = (x @ W).reshape(N, H, C)
        row, col = (edge_index[0], edge_index[1])
        a_src = att[0, :, :C]
        a_dst = att[0, :, C:]
        s_src = jnp.einsum('nhc,hc->nh', h, a_src)
        s_dst = jnp.einsum('nhc,hc->nh', h, a_dst)
        alpha = jax.nn.leaky_relu(s_src[row] + s_dst[col], negative_slope=0.2)
        seg_max = jax.ops.segment_max(alpha, row, num_segments=N)
        m = jnp.maximum(seg_max, 0.0)
        ex = jnp.exp(alpha - m[row])
        seg_sum = jax.ops.segment_sum(ex, row, num_segments=N)
        deg = jax.ops.segment_sum(jnp.ones((E,), x.dtype), row, num_segments=N)
        denom = seg_sum + (jnp.float32(E) - deg)[:, None] * jnp.exp(-m)
        alpha_n = ex / denom[row]
        msg = alpha_n[:, :, None] * h[col]
        out = jax.ops.segment_sum(msg, col, num_segments=N)
        out = out.reshape(N, H * C) + bias
        return out

    def _L1_gnn_ref(x, edge_index, edge_attr, W1, b1, W2, b2):
        import jax, jax.numpy as jnp
        import numpy as np
        N_NODES = 12500
        NODE_DIM = 128
        EDGE_DIM = 64
        HIDDEN_DIM = 256
        N_EDGES = 80000
        row = edge_index[0]
        col = edge_index[1]
        msg = jnp.concatenate([x[row], x[col], edge_attr], axis=-1)
        h = jax.nn.relu(msg @ W1 + b1)
        msg_out = h @ W2 + b2
        out = jax.ops.segment_sum(msg_out, row, num_segments=x.shape[0])
        return out
    edge_index = jnp.stack([src, dst])
    h = jnp.maximum(_layernorm(x, axis=-1), 0.0)
    x = x + _L0_gnn_ref(h, edge_index, L0_gnn_W, L0_gnn_att, L0_gnn_bias)
    h = jnp.maximum(_layernorm(x, axis=-1), 0.0)
    x = x + _L1_gnn_ref(h, edge_index, edge_attr_64, L1_gnn_W1, L1_gnn_b1, L1_gnn_W2, L1_gnn_b2)
    return x

_drawn_inputs = setup_inputs


def setup_inputs(seed=0):
    import zlib

    import numpy as np

    out = dict(_drawn_inputs(seed))
    spreads = {}
    factors = {'L0_gnn_W': 8.0,
     'L0_gnn_att': 8.0,
     'L0_gnn_bias': 58.971,
     'edge_attr_64': 2.831,
     'L1_gnn_b1': 4.114}
    for name, (base, spread) in spreads.items():
        noise = np.random.default_rng([zlib.crc32(name.encode()), seed]).standard_normal(out[name].shape)
        drawn = base * np.exp(spread * noise) if base else spread * noise
        out[name] = jnp.asarray(drawn.astype(out[name].dtype))
    for name, factor in factors.items():
        out[name] = (out[name] * factor).astype(out[name].dtype)
    return out
```

```python
from contextlib import ExitStack

import concourse.bass as bass
from concourse import mybir

F32 = mybir.dt.float32
BF16 = mybir.dt.bfloat16
I32 = mybir.dt.int32
ALU = mybir.AluOpType
ACT = mybir.ActivationFunctionType
X = mybir.AxisListType.X

P = 128
NODES, EDGES = 6250, 200000
D, HEADS, OC, ED, HID = 128, 4, 32, 64, 256
NB = -(-NODES // P)
NODES_P = NB * P
G = 8
GE = G * P
NG = -(-EDGES // GE)
EDGES_P = NG * GE
PAIR = 2 * P
NPAIR = (EDGES_P + NB * (PAIR - 1)) // PAIR
SLOTS = NPAIR * PAIR
TILES = SLOTS // P
NGS = TILES // G
EPS = 1e-5
SLOPE = 0.2
F_KEY, F_LOW, F_DST, F_SD, REC = ED, ED + 1, ED + 2, ED + 3, ED + 8
FILL = 26
HF = HEADS + 1
assert NPAIR % 4 == 0 and TILES % (2 * FILL) == 0 and NG % 2 == 0 and NGS % 2 == 0


def pairs(eng, body, n):
    body(0, 0)
    body(1, 1)
    with eng.Fori(1, n // 2) as i:
        body(i * 2, 0)
        body(i * 2 + 1, 1)
    if n % 2:
        body(n - 1, 0)


def first(k, n=1):
    return isinstance(k, int) and k < n


def freed(eng, sem, k, per=1):
    if not first(k, 2):
        eng.wait_ge(sem, (k - 1) * per)


class Chain:

    def __init__(self, eng, sem):
        self.eng, self.sem, self.n = eng, sem, 0

    def __call__(self, ins):
        self.n += 1
        ins.then_inc(self.sem, 1)
        self.eng.wait_ge(self.sem, self.n)


def row(ap, *dims):
    return ap.unsqueeze(1).to_broadcast(list(dims))


def col(ap, *dims):
    return ap.unsqueeze(len(dims) - 1).to_broadcast(list(dims))


def build(nc, x, src, dst, ea, W, att, bias, W1, b1, W2, b2, out):
    dram = lambda name, shape, dt: nc.dram_tensor(name, shape, dt).ap()
    rec_d = dram("rec_d", (SLOTS, REC), F32)
    head_d = dram("head_d", (SLOTS + NODES_P, HF), F32)
    low_src_d = dram("low_src_d", (EDGES_P,), BF16)
    low_dst_d = dram("low_dst_d", (EDGES_P,), BF16)
    low_row_d = dram("low_row_d", (SLOTS,), BF16)
    h_d = dram("h_d", (NODES_P, D), F32)
    x2_d = dram("x2_d", (NODES_P, D), F32)
    q_d = dram("q_d", (NODES_P, HID), F32)
    low_src_v, low_dst_v = (a.rearrange("(g p j) -> p g j", p=P, j=G) for a in (low_src_d, low_dst_d))
    src_v, dst_v = (a.rearrange("(g p j) -> p g j", p=P, j=G) for a in (src, dst))
    ea_v = ea.rearrange("(g p j) f -> g p j f", p=P, j=G)

    with ExitStack() as top:
        def sb(name, shape, dt, ctx=top):
            return ctx.enter_context(nc.sbuf_tensor(name, shape, dt))

        def pb(name, ctx, dt=F32):
            return ctx.enter_context(nc.psum_tensor(name, [P, 2048 // (4 if dt == F32 else 2)], dt))

        def sem(name):
            return top.enter_context(nc.semaphore(name))

        iota_i = sb("iota_i", [P, P], I32)
        part_i = sb("part_i", [P, 1], I32)
        iota = sb("iota", [P, P], F32)
        iota_b = sb("iota_b", [P, P], BF16)
        part = sb("part", [P, 1], F32)
        ident = sb("ident", [P, P], F32)
        below = sb("below", [P, P], F32)
        above = sb("above", [P, P], F32)
        ones = sb("ones", [P, P], F32)
        deg = sb("deg", [P, NB], F32)
        blk = sb("blk", [1, NPAIR], I32)
        wgt = sb("wgt", [P, HEADS, NB], F32)

        def normed_product(block, ctx, tag, xs, wx, ncol, ready, evacuate, follow=None):
            cent = sb(tag + "cent", [P, NB, D], F32, ctx)
            sq = sb(tag + "sq", [P, NB, D], F32, ctx)
            st = sb(tag + "st", [P, 4, NB], F32, ctx)
            hb = sb(tag + "hb", [P, 2, D], F32, ctx)
            hT = sb(tag + "hT", [P, 2, P], F32, ctx)
            tp = [pb(f"{tag}tp{k}", ctx) for k in range(2)]
            mp = [pb(f"{tag}mp{k}", ctx) for k in range(2)]
            s_var, s_std = sem(tag + "var_ready"), sem(tag + "std_ready")
            s_ch, s_h, s_t = sem(tag + "norm_chain"), sem(tag + "h_ready"), sem(tag + "h_turned")
            s_hT, s_mm, s_ev = sem(tag + "hT_ready"), sem(tag + "product_ready"), sem(tag + "product_moved")

            @block.vector
            def _(v):
                link = Chain(v, s_ch)
                ready(v)
                link(v.tensor_reduce(st[:, 0, :], xs[:, :, :], X, ALU.add))
                link(v.tensor_scalar(st[:, 1, :], st[:, 0, :], 1.0 / D, None, ALU.mult))
                link(v.tensor_tensor(cent[:, :, :], xs[:, :, :], col(st[:, 1, :], P, NB, D), ALU.subtract))
                link(v.tensor_tensor(sq[:, :, :], cent[:, :, :], cent[:, :, :], ALU.mult))
                link(v.tensor_reduce(st[:, 2, :], sq[:, :, :], X, ALU.add))
                v.tensor_scalar(st[:, 3, :], st[:, 2, :], 1.0 / D, EPS, ALU.mult, ALU.add).then_inc(s_var, 1)
                v.wait_ge(s_std, 1)
                link(v.reciprocal(st[:, 1, :], st[:, 0, :]))

                def normed(b, par):
                    freed(v, s_t, b)
                    v.tensor_scalar(hb[:, par, :], cent[:, bass.ds(b, 1), :].rearrange("p o d -> p (o d)"),
                                    st[:, 1, bass.ds(b, 1)], 0.0, ALU.mult, ALU.max).then_inc(s_h, 1)
                    if follow and not first(b):
                        follow(v, b - 1, 1 - par, s_ev)

                pairs(v, normed, NB)
                if follow:
                    follow(v, NB - 1, (NB - 1) % 2, s_ev)

            @block.tensor
            def _(pe):
                ready(pe)

                def product(b, par):
                    pe.wait_ge(s_h, b + 1)
                    freed(pe, s_hT, b)
                    pe.transpose(tp[par][:, 0:P], hb[:, par, :], ident[:, :]).then_inc(s_t, 1)
                    pe.wait_ge(s_hT, b + 1)
                    freed(pe, s_ev, b)
                    pe.matmul(mp[par][:, 0:ncol], hT[:, par, :], wx[:, 0:ncol], start=True, stop=True).then_inc(s_mm, 1)

                pairs(pe, product, NB)

            @block.scalar
            def _(act):
                act.wait_ge(s_var, 1)
                act.activation(st[:, 0, :], st[:, 3, :], ACT.Sqrt).then_inc(s_std, 1)

                def moved(b, par):
                    act.wait_ge(s_t, b + 1)
                    freed(act, s_mm, b)
                    act.activation(hT[:, par, :], tp[par][:, 0:P], ACT.Copy).then_inc(s_hT, 1)
                    act.wait_ge(s_mm, b + 1)
                    evacuate(act, b, par, mp[par], s_ev)

                pairs(act, moved, NB)

        with ExitStack() as edges:
            low_src = sb("low_src", [P, NG, G], BF16, edges)
            high_src = sb("high_src", [P, NG, G], BF16, edges)
            high_dst = sb("high_dst", [P, NG, G], BF16, edges)
            src_f = sb("src_f", [P, NG, G], F32, edges)
            dst_f = sb("dst_f", [P, NG, G], F32, edges)
            tab_sd = sb("tab_sd", [P, HEADS, NB], F32, edges)
            head = sb("head", [P, NB, HF], F32, edges)
            cnt = sb("cnt", [P, G, NB], F32, edges)
            head_i = sb("head_i", [P, NB], I32, edges)

            with ExitStack() as ctx:
                xs = sb("xs", [P, NB, D], F32, ctx)
                hrow = sb("hrow", [P, 2, D], F32, ctx)
                wx = sb("wx", [P, D + 2 * HEADS], F32, ctx)
                attb = sb("attb", [P, HEADS, 2, OC], F32, ctx)
                wa = sb("wa", [P, 2, HEADS, OC], F32, ctx)
                pad = sb("pad", [P, FILL, REC], F32, ctx)
                zero = sb("zero", [P, TILES * HF // 8], F32, ctx)
                ints = sb("ints", [P, 2, NG, G], I32, ctx)
                bits = sb("bits", [P, 4, NG, G], I32, ctx)
                low_dst = sb("low_dst", [P, NG, G], BF16, ctx)
                s_in, s_int, s_iota = sem("inputs"), sem("ints_loaded"), sem("iota_ready")
                s_c, s_wx, s_pad = sem("const_chain"), sem("wx_ready"), sem("pad_ready")
                s_fill, s_low, s_lowst, s_hst = sem("filled"), sem("low_ready"), sem("low_stored"), sem("h_stored")
                s_hs = [sem(f"h_row_stored{k}") for k in range(2)]
                block = ctx.enter_context(nc.Block())

                @block.sync
                def _(sp):
                    sp.dma_start(xs[:, :, :], x.rearrange("(b p) d -> p b d", p=P)).then_inc(s_in, 16)
                    sp.dma_start(wx[:, 0:D], W).then_inc(s_in, 16)
                    sp.dma_start(attb[:, :, :, :].rearrange("p h s c -> p (h s c)"),
                                 att.rearrange("o h c -> o (h c)").to_broadcast([P, 2 * HEADS * OC])).then_inc(s_in, 16)
                    sp.dma_start(ints[:, 0, :, :], src_v).then_inc(s_int, 16)
                    sp.dma_start(ints[:, 1, :, :], dst_v).then_inc(s_int, 16)
                    sp.wait_ge(s_pad, 2)
                    for k in range(8):
                        n = TILES * HF // 8
                        sp.dma_start(head_d[0:SLOTS, :].rearrange("(p c) f -> p (c f)", p=P)[:, k * n:(k + 1) * n],
                                     zero[:, :]).then_inc(s_fill, 16)
                    rows = rec_d.rearrange("(p k c) f -> k p (c f)", p=P, c=FILL)
                    with sp.Fori(0, TILES // FILL) as k:
                        sp.dma_start(rows[bass.ds(k, 1), :, :].rearrange("o p n -> (o p) n"),
                                     pad[:, :, :].rearrange("p c f -> p (c f)")).then_inc(s_fill, 16)
                    sp.wait_ge(s_low, 1)
                    sp.dma_start(low_src_v, low_src[:, :, :]).then_inc(s_lowst, 16)
                    sp.dma_start(low_dst_v, low_dst[:, :, :]).then_inc(s_lowst, 16)
                    sp.wait_ge(s_lowst, 32)
                    sp.wait_ge(s_fill, 16 * (8 + TILES // FILL))

                @block.gpsimd
                def _(pool):
                    pool.iota(iota_i[:, :], [[1, P]], base=0, channel_multiplier=0).then_inc(s_iota, 1)
                    pool.iota(part_i[:, :], [[0, 1]], base=0, channel_multiplier=1).then_inc(s_iota, 1)
                    pool.memset(ones[:, :], 1.0).then_inc(s_iota, 1)
                    pool.memset(pad[:, :, :], 0.0).then_inc(s_iota, 1)
                    pool.memset(zero[:, :], 0.0).then_inc(s_pad, 1)
                    pool.wait_ge(s_iota, 4)
                    pool.memset(pad[:, :, F_KEY:F_DST + 1], -1.0).then_inc(s_pad, 1)

                @block.vector
                def _(v):
                    link = Chain(v, s_c)
                    v.wait_ge(s_iota, 2)
                    v.tensor_copy(iota_b[:, :], iota_i[:, :])
                    v.tensor_copy(iota[:, :], iota_i[:, :])
                    link(v.tensor_copy(part[:, :], part_i[:, :]))
                    v.tensor_scalar(below[:, :], iota[:, :], part[:, 0:1], None, ALU.is_lt)
                    v.tensor_scalar(above[:, :], iota[:, :], part[:, 0:1], None, ALU.is_gt)
                    link(v.tensor_scalar(ident[:, :], iota[:, :], part[:, 0:1], None, ALU.is_equal))
                    v.wait_ge(s_in, 48)
                    for s in range(2):
                        v.tensor_tensor(wa[:, s, :, :], wx[:, 0:D].rearrange("p (h c) -> p h c", h=HEADS),
                                        attb[:, :, s, :], ALU.mult)
                    link(v.memset(head[:, :, :], 0.0))
                    v.tensor_reduce(wx[:, D:D + 2 * HEADS], wa[:, :, :, :].rearrange("p s h c -> p (s h) c"),
                                    X, ALU.add).then_inc(s_wx, 1)
                    v.wait_ge(s_int, 32)
                    v.tensor_copy(src_f[:, :, :], ints[:, 0, :, :])
                    v.tensor_copy(dst_f[:, :, :], ints[:, 1, :, :])
                    for k in range(2):
                        v.tensor_scalar(bits[:, 2 * k, :, :], ints[:, k, :, :], P - 1, None, ALU.bitwise_and)
                        link(v.tensor_scalar(bits[:, 2 * k + 1, :, :], ints[:, k, :, :], 7, None, ALU.arith_shift_right))
                    v.tensor_copy(high_src[:, :, :], bits[:, 1, :, :])
                    v.tensor_copy(high_dst[:, :, :], bits[:, 3, :, :])
                    v.tensor_copy(low_src[:, :, :], bits[:, 0, :, :])
                    v.tensor_copy(low_dst[:, :, :], bits[:, 2, :, :]).then_inc(s_low, 1)

                def ready(eng):
                    eng.wait_ge(s_wx, 1)
                    eng.wait_ge(s_in, 48)

                def evacuate(act, b, par, ps, moved):
                    if not first(b, 2):
                        act.wait_ge(s_hs[par], (b - par) * 8)
                    act.activation(hrow[:, par, :], ps[:, 0:D], ACT.Copy).then_inc(s_hst, 1)
                    act.activation(head[:, bass.ds(b, 1), 0:HEADS].rearrange("p o h -> p (o h)"), ps[:, D:D + HEADS], ACT.Copy)
                    act.activation(tab_sd[:, :, bass.ds(b, 1)].rearrange("p h o -> p (h o)"),
                                   ps[:, D + HEADS:D + 2 * HEADS], ACT.Copy).then_inc(moved, 1)
                    act.wait_ge(s_hst, b + 1)
                    act.dma_start(h_d.rearrange("(b p) d -> b p d", p=P)[bass.ds(b, 1), :, :].rearrange("o p d -> (o p) d"),
                                  hrow[:, par, :]).then_inc(s_hs[par], 16)

                normed_product(block, ctx, "l0_", xs, wx, D + 2 * HEADS, ready, evacuate)

                @block.scalar
                def _(act):
                    act.wait_ge(s_hs[0], 16 * (NB - NB // 2))
                    act.wait_ge(s_hs[1], 16 * (NB // 2))

            with ExitStack() as ctx:
                oh_low = sb("oh_low", [P, 2, G, P], BF16, ctx)
                oh_high = sb("oh_high", [P, 2, G, NB], BF16, ctx)
                hist = [pb(f"hist{k}", ctx) for k in range(2)]
                s_oh, s_hist, s_cnt = sem("pre_onehot_ready"), sem("pre_hist_ready"), sem("count_added")
                block = ctx.enter_context(nc.Block())

                @block.vector
                def _(v):
                    v.memset(cnt[:, :, :], 0.0).then_inc(s_cnt, 1)

                    def add(g, par):
                        v.wait_ge(s_hist, g + 1)
                        v.wait_ge(s_cnt, g + 1)
                        v.tensor_tensor(cnt[:, :, :].rearrange("p s a -> p (s a)"), cnt[:, :, :].rearrange("p s a -> p (s a)"),
                                        hist[par][:, 0:G * NB], ALU.add).then_inc(s_cnt, 1)

                    def onehot(g, par):
                        freed(v, s_hist, g)
                        v.tensor_tensor(oh_low[:, par, :, :], col(low_src[:, bass.ds(g, 1), :].rearrange("p o j -> p (o j)"), P, G, P),
                                        row(iota_b[:, :], P, G, P), ALU.is_equal)
                        v.tensor_tensor(oh_high[:, par, :, :], col(high_src[:, bass.ds(g, 1), :].rearrange("p o j -> p (o j)"), P, G, NB),
                                        row(iota_b[:, 0:NB], P, G, NB), ALU.is_equal).then_inc(s_oh, 1)
                        if not first(g):
                            add(g - 1, 1 - par)

                    pairs(v, onehot, NG)
                    add(NG - 1, (NG - 1) % 2)

                @block.tensor
                def _(pe):
                    def count(g, par):
                        pe.wait_ge(s_oh, g + 1)
                        if not first(g, 2):
                            pe.wait_ge(s_cnt, g)
                        for j in range(G):
                            mm = pe.matmul(hist[par][:, j * NB:(j + 1) * NB], oh_low[:, par, j, :], oh_high[:, par, j, :],
                                           start=True, stop=True)
                        mm.then_inc(s_hist, 1)

                    pairs(pe, count, NG)

            with ExitStack() as ctx:
                t = sb("t", [P, 8, NB], F32, ctx)
                ti = sb("ti", [P, 2, NB], I32, ctx)
                excl = sb("excl", [P, G, NB], F32, ctx)
                pair_i = sb("pair_i", [P, NPAIR], I32, ctx)
                pair_f = sb("pair_f", [P, NPAIR], F32, ctx)
                blk_f = sb("blk_f", [1, NPAIR], F32, ctx)
                sums = pb("sums", ctx)
                bp = [pb(f"bp{k}", ctx) for k in range(2)]
                s_b, s_deg, s_sum = sem("base_chain"), sem("degree_ready"), sem("sums_ready")
                s_pi, s_ge, s_bp = sem("pair_iota"), sem("pair_compared"), sem("pair_block_ready")
                block = ctx.enter_context(nc.Block())

                @block.gpsimd
                def _(pool):
                    pool.iota(pair_i[:, :], [[1, NPAIR]], base=0, channel_multiplier=0).then_inc(s_pi, 1)

                @block.vector
                def _(v):
                    link = Chain(v, s_b)
                    link(v.memset(excl[:, 0, :], 0.0))
                    for s in range(1, G):
                        link(v.tensor_tensor(excl[:, s, :], excl[:, s - 1, :], cnt[:, s - 1, :], ALU.add))
                    v.tensor_tensor(deg[:, :], excl[:, G - 1, :], cnt[:, G - 1, :], ALU.add).then_inc(s_deg, 1)
                    v.wait_ge(s_sum, 2)
                    start, total = sums[:, 0:NB], sums[:, NB:2 * NB]
                    link(v.tensor_scalar(ti[:, 0, :], total, float(PAIR - 1), None, ALU.add))
                    link(v.tensor_scalar(ti[:, 1, :], ti[:, 0, :], PAIR.bit_length() - 1, None, ALU.arith_shift_right))
                    link(v.tensor_copy(t[:, 0, :], ti[:, 1, :]))
                    link(v.tensor_tensor_scan(t[:, 1, :], ones[:, 0:NB], t[:, 0, :], 0.0, ALU.mult, ALU.add))
                    link(v.tensor_tensor(t[:, 2, :], t[:, 1, :], t[:, 0, :], ALU.subtract))
                    link(v.tensor_scalar(t[:, 3, :], t[:, 2, :], float(PAIR), None, ALU.mult))
                    link(v.tensor_tensor(t[:, 4, :], t[:, 3, :], start, ALU.add))
                    for s in range(G):
                        v.tensor_tensor(cnt[:, s, :], excl[:, s, :], t[:, 4, :], ALU.add)
                    link(v.tensor_scalar(t[:, 5, :], deg[:, :], 0.0, None, ALU.is_equal))
                    link(v.tensor_scalar(t[:, 6, :], iota[:, 0:NB], float(P), part[:, 0:1], ALU.mult, ALU.add))
                    link(v.tensor_scalar(t[:, 6, :], t[:, 6, :], float(SLOTS), None, ALU.add))
                    link(v.tensor_tensor(t[:, 6, :], t[:, 6, :], t[:, 4, :], ALU.subtract))
                    link(v.tensor_tensor(t[:, 6, :], t[:, 6, :], t[:, 5, :], ALU.mult))
                    link(v.tensor_tensor(head_i[:, :], t[:, 6, :], t[:, 4, :], ALU.add))
                    link(v.tensor_copy(head[:, :, HEADS], deg[:, :]))
                    link(v.tensor_tensor(t[:, 7, :], t[:, 1, :], ident[:, 0:NB], ALU.mult))
                    link(v.tensor_reduce(t[:, 0, 0:1], t[:, 7, :], X, ALU.add))
                    v.wait_ge(s_pi, 1)
                    v.tensor_scalar(pair_f[:, :], pair_i[:, :], t[:, 0, 0:1], None, ALU.is_ge).then_inc(s_ge, 1)
                    v.wait_ge(s_bp, 1)
                    half = NPAIR // 2
                    for k in range(2):
                        link(v.tensor_scalar(blk[:, k * half:(k + 1) * half], bp[k][0:1, 0:half], float(NB - 1), None, ALU.min))

                @block.tensor
                def _(pe):
                    pe.wait_ge(s_deg, 1)
                    pe.matmul(sums[:, 0:NB], above[:, :], deg[:, :], start=True, stop=True).then_inc(s_sum, 1)
                    pe.matmul(sums[:, NB:2 * NB], ones[:, :], deg[:, :], start=True, stop=True).then_inc(s_sum, 1)
                    pe.wait_ge(s_ge, 1)
                    half = NPAIR // 2
                    for k in range(2):
                        mm = pe.matmul(bp[k][0:1, 0:half], ones[0:NB, 0:1], pair_f[0:NB, k * half:(k + 1) * half],
                                       start=True, stop=True)
                    mm.then_inc(s_bp, 1)

            with ExitStack() as ctx:
                oh_low = sb("c_oh_low", [P, 2, G, P], BF16, ctx)
                oh_high = sb("c_oh_high", [P, 2, G, NB], BF16, ctx)
                oh_dst = sb("c_oh_dst", [P, 2, G, NB], BF16, ctx)
                src_row = sb("src_row", [P, 2, P, G], I32, ctx)
                lsrc_row = sb("lsrc_row", [P, 2, P, G], BF16, ctx)
                ldst_row = sb("ldst_row", [P, 2, P, G], BF16, ctx)
                ohT_src = sb("ohT_src", [P, 2, P, G], F32, ctx)
                ohT_dst = sb("ohT_dst", [P, 2, P, G], F32, ctx)
                same = sb("same", [P, G, P], F32, ctx)
                rank = sb("rank", [P, 2, G], F32, ctx)
                pick = sb("pick", [P, G, NB], F32, ctx)
                minus_part = sb("minus_part", [P, 1], F32, ctx)
                one_col = sb("one_col", [P, 1], F32, ctx)
                picked = sb("picked", [P, G], F32, ctx)
                pick_sd = sb("pick_sd", [P, G, HEADS, NB], F32, ctx)
                place = sb("place", [P, 2, G], I32, ctx)
                rec = sb("rec", [P, 2, G, REC], F32, ctx)
                hist = [pb(f"c_hist{k}", ctx) for k in range(2)]
                pos_ps = [pb(f"pos_ps{k}", ctx) for k in range(2)]
                sd_ps = [pb(f"sd_ps{k}", ctx) for k in range(4)]
                s_ld = [sem(f"group_loaded{k}") for k in range(2)]
                s_sc = [sem(f"group_scattered{k}") for k in range(2)]
                s_away = sem("distances_ready")
                s_z, s_oh, s_ohT, s_eq = sem("rec_zeroed"), sem("onehot_ready"), sem("onehotT_ready"), sem("rank_ready")
                s_hist, s_tab, s_pos, s_sd = sem("hist_ready"), sem("table_moved"), sem("start_looked_up"), sem("score_looked_up")
                s_pick, s_picked, s_picksd, s_rec = sem("start_masked"), sem("start_picked"), sem("score_masked"), sem("record_ready")
                s_heads, s_go = sem("heads_scattered"), sem("scatter_begun")
                s_ea = [sem(f"attributes_loaded{k}") for k in range(2)]
                block = ctx.enter_context(nc.Block())

                @block.sync
                def _(sp):
                    def load(g, par):
                        if not first(g, 2):
                            sp.wait_ge(s_eq, g - 1)
                            sp.wait_ge(s_ohT, g - 1)
                        one = bass.ds(g, 1)
                        for to, of in ((src_row, src), (lsrc_row, low_src_d), (ldst_row, low_dst_d)):
                            sp.dma_start(to[:, par, :, :].rearrange("p q j -> p (q j)"),
                                         of.rearrange("(g e) -> g e", e=GE)[one, :].to_broadcast([P, GE])).then_inc(s_ld[par], 16)

                    pairs(sp, load, NG)

                @block.scalar
                def _(act):
                    def turned_onehots(g, par):
                        act.wait_ge(s_ld[par], (g - par) * 24 + 48)
                        if not first(g, 2):
                            act.wait_ge(s_sd, (g - 1) * 4)
                        for oh, low in ((ohT_src, lsrc_row), (ohT_dst, ldst_row)):
                            act.activation(oh[:, par, :, :], low[:, par, :, :], ACT.Abs, bias=minus_part[:, 0:1]
                                           ).then_inc(s_away, 1)
                        for k, oh in enumerate((ohT_src, ohT_dst)):
                            act.wait_ge(s_away, g * 2 + (k + 1))
                            ins = act.activation(oh[:, par, :, :], oh[:, par, :, :], ACT.Relu, bias=one_col[:, 0:1], scale=-1.0)
                        ins.then_inc(s_ohT, 1)

                    def load(g, par):
                        turned_onehots(g, par)
                        if not first(g, 2):
                            act.wait_ge(s_sc[par], (g - par) * (8 * G))
                        act.dma_start(rec[:, par, :, 0:ED], ea_v[bass.ds(g, 1), :, :, :].rearrange("o p j f -> (o p) j f")
                                      ).then_inc(s_ea[par], 16)

                    act.wait_ge(s_z, 1)
                    pairs(act, load, NG)

                @block.gpsimd
                def _(pool):
                    for a in range(NB):
                        pool.indirect_dma_start(head_d, bass.IndirectOffsetOnAxis(ap=head_i[:, a:a + 1], axis=0),
                                                head[:, a, :], None).then_inc(s_heads, 16)

                    def scatter(g, par):
                        pool.wait_ge(s_rec, g + 1)
                        pool.wait_ge(s_ea[par], (g - par) * 8 + 16)
                        pool.sem_inc(s_go, 1)
                        for j in range(G):
                            pool.indirect_dma_start(rec_d, bass.IndirectOffsetOnAxis(ap=place[:, par, j:j + 1], axis=0),
                                                    rec[:, par, j, :], None).then_inc(s_sc[par], 16)

                    pairs(pool, scatter, NG)
                    pool.wait_ge(s_heads, 16 * NB)
                    pool.wait_ge(s_sc[0], 8 * G * NG)
                    pool.wait_ge(s_sc[1], 8 * G * NG)

                @block.vector
                def _(v):
                    v.tensor_scalar(minus_part[:, :], part[:, 0:1], -1.0, None, ALU.mult)
                    v.memset(one_col[:, :], 1.0)
                    v.memset(rec[:, :, :, :], 0.0).then_inc(s_z, 1)

                    def prepare(g, par):
                        one = bass.ds(g, 1)
                        tile = lambda a: a[:, one, :].rearrange("p o j -> p (o j)")
                        freed(v, s_hist, g)
                        v.tensor_tensor(oh_low[:, par, :, :], col(tile(low_src), P, G, P), row(iota_b[:, :], P, G, P), ALU.is_equal)
                        v.tensor_tensor(oh_high[:, par, :, :], col(tile(high_src), P, G, NB), row(iota_b[:, 0:NB], P, G, NB),
                                        ALU.is_equal).then_inc(s_oh, 1)
                        v.wait_ge(s_ld[par], (g - par) * 24 + 48)
                        v.tensor_tensor(oh_dst[:, par, :, :], col(tile(high_dst), P, G, NB), row(iota_b[:, 0:NB], P, G, NB), ALU.is_equal)
                        if not first(g):
                            v.wait_ge(s_eq, g)
                        freed(v, s_rec, g)
                        for j in range(G):
                            eq = v.scalar_tensor_tensor(out=same[:, j, :], in0=src_row[:, par, :, j],
                                                        scalar=src_f[:, one, j:j + 1].rearrange("p o j -> p (o j)"),
                                                        in1=below[:, :], op0=ALU.is_equal, op1=ALU.mult,
                                                        accum_out=rank[:, par, j:j + 1])
                        eq.then_inc(s_eq, 1)
                        if not first(g):
                            v.wait_ge(s_hist, g)
                            v.wait_ge(s_pos, g)
                            if not first(g, 2):
                                v.wait_ge(s_tab, g - 1)
                            v.tensor_tensor(cnt[:, :, :].rearrange("p s a -> p (s a)"), cnt[:, :, :].rearrange("p s a -> p (s a)"),
                                            hist[1 - par][:, 0:G * NB], ALU.add).then_inc(s_tab, 1)

                    def finish(g, par):
                        one = bass.ds(g, 1)
                        v.wait_ge(s_pos, g + 1)
                        if not first(g):
                            v.wait_ge(s_picked, g)
                        v.tensor_tensor(pick[:, :, :], pos_ps[par][:, 0:G * NB].rearrange("p (j a) -> p j a", j=G),
                                        oh_high[:, par, :, :], ALU.mult).then_inc(s_pick, 1)
                        for q in range(4):
                            v.wait_ge(s_sd, g * 4 + (q + 1))
                            if q == 0 and not first(g):
                                v.wait_ge(s_rec, g)
                            for k in range(2):
                                ins = v.tensor_tensor(
                                    pick_sd[:, 2 * q + k, :, :],
                                    sd_ps[q][:, k * HEADS * NB:(k + 1) * HEADS * NB].rearrange("p (h a) -> p h a", h=HEADS),
                                    row(oh_dst[:, par, 2 * q + k, :], P, HEADS, NB), ALU.mult)
                            ins.then_inc(s_picksd, 1)
                        v.wait_ge(s_pick, g + 1)
                        v.tensor_reduce(picked[:, :], pick[:, :, :], X, ALU.add).then_inc(s_picked, 1)
                        v.wait_ge(s_picksd, g * 4 + 4)
                        if not first(g, 2):
                            v.wait_ge(s_sc[par], (g - par) * (8 * G))
                        v.tensor_reduce(rec[:, par, :, F_SD:F_SD + HEADS], pick_sd[:, :, :, :], X, ALU.add)
                        for f, of in ((F_KEY, src_f), (F_LOW, low_src), (F_DST, dst_f)):
                            v.tensor_copy(rec[:, par, :, f], of[:, one, :].rearrange("p o j -> p (o j)"))
                        v.wait_ge(s_picked, g + 1)
                        v.wait_ge(s_eq, g + 1)
                        v.tensor_tensor(place[:, par, :], picked[:, :], rank[:, par, :], ALU.add).then_inc(s_rec, 1)

                    v.wait_ge(s_z, 1)
                    prepare(0, 0)
                    prepare(1, 1)
                    finish(0, 0)
                    prepare(2, 0)
                    finish(1, 1)
                    with v.Fori(1, NG // 2 - 1) as i:
                        prepare(i * 2 + 1, 1)
                        finish(i * 2, 0)
                        prepare(i * 2 + 2, 0)
                        finish(i * 2 + 1, 1)
                    prepare(NG - 1, 1)
                    finish(NG - 2, 0)
                    finish(NG - 1, 1)

                @block.tensor
                def _(pe):
                    def look_up(g, par):
                        pe.wait_ge(s_oh, g + 1)
                        if not first(g, 2):
                            pe.wait_ge(s_tab, g - 1)
                        for j in range(G):
                            mm = pe.matmul(hist[par][:, j * NB:(j + 1) * NB], oh_low[:, par, j, :], oh_high[:, par, j, :],
                                           start=True, stop=True)
                        mm.then_inc(s_hist, 1)
                        pe.wait_ge(s_ohT, g + 1)
                        if not first(g):
                            pe.wait_ge(s_tab, g)
                        freed(pe, s_pick, g)
                        for j in range(G):
                            mm = pe.matmul(pos_ps[par][:, j * NB:(j + 1) * NB], ohT_src[:, par, :, j], cnt[:, j, :],
                                           start=True, stop=True)
                        mm.then_inc(s_pos, 1)
                        for q in range(4):
                            if not first(g):
                                pe.wait_ge(s_picksd, (g - 1) * 4 + (q + 1))
                            for k in range(2):
                                mm = pe.matmul(sd_ps[q][:, k * HEADS * NB:(k + 1) * HEADS * NB], ohT_dst[:, par, :, 2 * q + k],
                                               tab_sd[:, :, :].rearrange("p h a -> p (h a)"), start=True, stop=True)
                            mm.then_inc(s_sd, 1)

                    pairs(pe, look_up, NG)

        with ExitStack() as soft:
            S = TILES
            fld = sb("fld", [P, S, F_SD + HEADS - F_KEY], F32, soft)
            al = sb("al", [P, HEADS, S], F32, soft)
            low_dst = sb("s_low_dst", [P, S], BF16, soft)
            high_dst = sb("s_high_dst", [P, S], BF16, soft)
            with ExitStack() as ctx:
                hd = sb("hd", [P, S, HF], F32, ctx)
                sc = sb("sc", [P, HEADS, S], F32, ctx)
                dg = sb("dg", [P, S], F32, ctx)
                fwd = sb("fwd", [P, S + 1], F32, ctx)
                edge = sb("edge", [P, 2], F32, ctx)
                ends = sb("ends", [P, 2, HF], F32, ctx)
                full = sb("full", [P, 2], F32, ctx)
                endsT = sb("endsT", [HF, 2, P], F32, ctx)
                carT = sb("carT", [HF, P + 2], F32, ctx)
                car = sb("car", [P, HF], F32, ctx)
                lowrow = sb("lowrow", [P, S], BF16, ctx)
                tps = [pb(f"carry{k}", ctx) for k in range(3)]
                s_in, s_ch, s_e0 = sem("sorted_loaded"), sem("softmax_chain"), sem("edge_zeroed")
                s_endr, s_endt, s_carr, s_cart = sem("ends_ready"), sem("ends_turned"), sem("carry_ready"), sem("carry_turned")
                s_mr, s_exp = sem("max_ready"), sem("exp_ready")
                s_lr, s_ls = sem("lowrow_ready"), sem("lowrow_stored")
                NSCAN = 5
                block = ctx.enter_context(nc.Block())
                recs = rec_d.rearrange("(p c) f -> p c f", p=P)

                @block.sync
                def _(sp):
                    sp.dma_start(fld[:, :, :], recs[:, :, F_KEY:F_SD + HEADS]).then_inc(s_in, 16)
                    sp.dma_start(hd[:, :, :], head_d[0:SLOTS, :].rearrange("(p c) f -> p c f", p=P)).then_inc(s_in, 16)
                    sp.wait_ge(s_e0, 1)
                    sp.dma_start(edge[1:P, 0:1], recs[0:P - 1, S - 1, F_KEY:F_KEY + 1],
                                 allow_slow_non_contiguous=True).then_inc(s_in, 16)
                    sp.dma_start(edge[0:P - 1, 1:2], recs[1:P, 0, F_KEY:F_KEY + 1],
                                 allow_slow_non_contiguous=True).then_inc(s_in, 16)
                    sp.wait_ge(s_lr, 1)
                    sp.dma_start(low_row_d.rearrange("(p c) -> p c", p=P), lowrow[:, :]).then_inc(s_ls, 16)
                    sp.wait_ge(s_ls, 16)

                @block.tensor
                def _(pe):
                    for k in range(NSCAN):
                        pe.wait_ge(s_endr, k + 1)
                        pe.transpose(tps[0][0:HF, 0:P], ends[:, 0, :], ident[:, :])
                        pe.transpose(tps[1][0:HF, 0:P], ends[:, 1, :], ident[:, :]).then_inc(s_endt, 1)
                        pe.wait_ge(s_carr, k + 1)
                        pe.transpose(tps[2][:, 0:HF], carT[:, 1:P + 1], ident[0:HF, 0:HF]).then_inc(s_cart, 1)

                @block.scalar
                def _(act):
                    for n in range(2):
                        act.wait_ge(s_mr, n + 1)
                        if n == 0:
                            e = act.activation(al[:, :, :], al[:, :, :], ACT.Exp)
                        else:
                            e = act.activation(sc[:, :, :], sc[:, :, :], ACT.Exp, scale=-1.0)
                        e.then_inc(s_exp, 1)

                @block.vector
                def _(v):
                    link = Chain(v, s_ch)
                    link(v.memset(edge[:, :], -2.0))
                    v.memset(carT[:, :], 0.0)
                    v.memset(ends[:, :, :], 0.0).then_inc(s_e0, 1)
                    v.wait_ge(s_e0, 1)
                    v.wait_ge(s_in, 64)
                    key = fld[:, :, 0]
                    v.tensor_tensor(fwd[:, 1:S], fld[:, 1:S, 0], fld[:, 0:S - 1, 0], ALU.is_equal)
                    v.tensor_tensor(fwd[:, 0:1], edge[:, 0:1], fld[:, 0:1, 0], ALU.is_equal)
                    link(v.tensor_tensor(fwd[:, S:S + 1], edge[:, 1:2], fld[:, S - 1:S, 0], ALU.is_equal))
                    v.tensor_reduce(full[:, 0:1], fwd[:, 0:S], X, ALU.min)
                    link(v.tensor_reduce(full[:, 1:2], fwd[:, 1:S + 1], X, ALU.min))
                    v.tensor_copy(lowrow[:, :], fld[:, :, 1]).then_inc(s_lr, 1)

                    def segments(k, outs, datas, op, back):
                        n = len(outs)
                        d = 1 if back else 0
                        turn = (lambda a: a[:, ::-1]) if back else (lambda a: a)
                        flag = turn(fwd[:, 1:S + 1] if back else fwd[:, 0:S])
                        for o, a in zip(outs, datas):
                            ins = v.tensor_tensor_scan(turn(o), flag, turn(a), 0.0, ALU.mult, op)
                        link(ins)
                        for c, o in enumerate(outs):
                            v.tensor_copy(ends[:, 0, c:c + 1], o[:, 0:1] if back else o[:, S - 1:S])
                        v.tensor_copy(ends[:, 1, :], full[:, d:d + 1].to_broadcast([P, HF])).then_inc(s_endr, 1)
                        v.wait_ge(s_endt, k + 1)
                        v.tensor_copy(endsT[:, 0, :], tps[0][0:HF, 0:P])
                        link(v.tensor_copy(endsT[:, 1, :], tps[1][0:HF, 0:P]))
                        if back:
                            link(v.memset(carT[:, P:P + 1], 0.0))
                            v.tensor_tensor_scan(carT[:, 0:P][:, ::-1], endsT[:, 1, ::-1], endsT[:, 0, ::-1], 0.0,
                                                 ALU.mult, op).then_inc(s_carr, 1)
                        else:
                            link(v.memset(carT[:, 1:2], 0.0))
                            v.tensor_tensor_scan(carT[:, 2:P + 2], endsT[:, 1, :], endsT[:, 0, :], 0.0,
                                                 ALU.mult, op).then_inc(s_carr, 1)
                        v.wait_ge(s_cart, k + 1)
                        link(v.tensor_copy(car[:, :], tps[2][:, 0:HF]))
                        for c, (o, a) in enumerate(zip(outs, datas)):
                            ins = v.tensor_tensor_scan(turn(o), flag, turn(a), car[:, c:c + 1], ALU.mult, op)
                        link(ins)

                    heads = lambda a: [a[:, h, :] for h in range(HEADS)]
                    hds = [hd[:, :, h] for h in range(HEADS)]
                    segments(0, heads(al) + [dg[:, :]], hds + [hd[:, :, HEADS]], ALU.add, False)
                    link(v.tensor_tensor(al[:, :, :], al[:, :, :], fld[:, :, 3:3 + HEADS].rearrange("p c h -> p h c"), ALU.add))
                    for h in range(HEADS):
                        ins = v.scalar_tensor_tensor(out=al[:, h, :], in0=al[:, h, :], scalar=SLOPE, in1=al[:, h, :],
                                                     op0=ALU.mult, op1=ALU.max)
                    link(ins)
                    segments(1, hds, heads(al), ALU.max, False)
                    segments(2, heads(sc), hds, ALU.max, True)
                    v.tensor_tensor(al[:, :, :], al[:, :, :], sc[:, :, :], ALU.subtract).then_inc(s_mr, 1)
                    v.wait_ge(s_exp, 1)
                    v.wait_ge(s_mr, 1)
                    v.engine_nop().then_inc(s_mr, 1)
                    v.wait_ge(s_exp, 2)
                    link(v.tensor_scalar(dg[:, :], dg[:, :], -1.0, float(EDGES), ALU.mult, ALU.add))
                    link(v.tensor_tensor(sc[:, :, :], sc[:, :, :], row(dg[:, :], P, HEADS, S), ALU.mult))
                    segments(3, hds, heads(al), ALU.add, False)
                    tot = [fld[:, :, 3 + h] for h in range(HEADS)]
                    segments(4, tot, hds, ALU.max, True)
                    link(v.tensor_tensor(sc[:, :, :], sc[:, :, :], fld[:, :, 3:3 + HEADS].rearrange("p c h -> p h c"), ALU.add))
                    link(v.reciprocal(sc[:, :, :], sc[:, :, :]))
                    link(v.tensor_tensor(al[:, :, :], al[:, :, :], sc[:, :, :], ALU.mult))
                    bits = hd[:, :, 0:2].bitcast(I32)
                    link(v.tensor_copy(bits[:, :, 0], fld[:, :, 2]))
                    link(v.tensor_scalar(bits[:, :, 1], bits[:, :, 0], P - 1, None, ALU.bitwise_and))
                    link(v.tensor_copy(low_dst[:, :], bits[:, :, 1]))
                    link(v.tensor_scalar(bits[:, :, 1], bits[:, :, 0], 7, None, ALU.arith_shift_right))
                    link(v.tensor_copy(high_dst[:, :], bits[:, :, 1]))

            with ExitStack() as ctx:
                oh_low = sb("e_oh_low", [P, 2, G, P], F32, ctx)
                oh_high = sb("e_oh_high", [P, 2, G, NB], F32, ctx)
                oh_w = sb("e_oh_w", [P, 2, G, HEADS, NB], F32, ctx)
                acc = pb("e_acc", ctx)
                s_hi, s_w, s_acc = sem("e_high_ready"), sem("e_weights_ready"), sem("e_multiplied")
                s_out = sem("e_moved")
                block = ctx.enter_context(nc.Block())

                @block.vector
                def _(v):
                    def weigh(g, par):
                        tile = lambda a: a[:, bass.ds(g * G, G)]
                        freed(v, s_acc, g)
                        v.tensor_tensor(oh_high[:, par, :, :], col(tile(high_dst), P, G, NB), row(iota_b[:, 0:NB], P, G, NB),
                                        ALU.is_equal).then_inc(s_hi, 1)
                        v.tensor_tensor(oh_low[:, par, :, :], col(tile(low_dst), P, G, P), row(iota_b[:, :], P, G, P), ALU.is_equal)
                        v.wait_ge(s_hi, g + 1)
                        for h in range(HEADS):
                            ins = v.tensor_tensor(oh_w[:, par, :, h, :], oh_high[:, par, :, :],
                                                  col(al[:, h, bass.ds(g * G, G)], P, G, NB), ALU.mult)
                        ins.then_inc(s_w, 1)

                    pairs(v, weigh, NGS)
                    v.wait_ge(s_acc, NGS)
                    v.tensor_copy(wgt[:, :, :].rearrange("p h a -> p (h a)"), acc[:, 0:HEADS * NB]).then_inc(s_out, 1)

                @block.tensor
                def _(pe):
                    def gather(g, par):
                        pe.wait_ge(s_w, g + 1)
                        for j in range(G):
                            mm = pe.matmul(acc[:, 0:HEADS * NB], oh_low[:, par, j, :],
                                           oh_w[:, par, j, :, :].rearrange("p h a -> p (h a)"),
                                           start=first(g) and j == 0, stop=isinstance(g, int) and g == NGS - 1 and j == G - 1,
                                           skip_group_check=True)
                        mm.then_inc(s_acc, 1)

                    pairs(pe, gather, NGS)

        pn = sb("pn", [P, NB, 3, HID], BF16)
        with ExitStack() as ctx:
            bias_b = sb("bias_b", [P, D], F32, ctx)
            b1_b = sb("b1_b", [P, HID], F32, ctx)
            w1 = sb("w1", [P, 2, HID], F32, ctx)
            qrow = sb("qrow", [P, 2, HID], F32, ctx)
            prow = sb("prow", [P, 2, HID], F32, ctx)
            x2 = sb("x2", [P, NB, D], F32, ctx)
            s_in, s_ch, s_x2 = sem("l1_inputs"), sem("x2_chain"), sem("x2_ready")
            with ExitStack() as c2:
                hh = sb("hh", [P, NB, D], F32, c2)
                block = c2.enter_context(nc.Block())

                @block.sync
                def _(sp):
                    sp.dma_start(x2[:, :, :], x.rearrange("(b p) d -> p b d", p=P)).then_inc(s_in, 16)
                    sp.dma_start(hh[:, :, :], h_d.rearrange("(b p) d -> p b d", p=P)).then_inc(s_in, 16)
                    sp.dma_start(bias_b[:, :], bias.rearrange("(o f) -> o f", o=1).to_broadcast([P, D])).then_inc(s_in, 16)
                    sp.dma_start(b1_b[:, :], b1.rearrange("(o f) -> o f", o=1).to_broadcast([P, HID])).then_inc(s_in, 16)
                    sp.dma_start(w1[:, :, :], W1[0:2 * D, :].rearrange("(s d) f -> d s f", s=2)).then_inc(s_in, 16)
                    sp.wait_ge(s_in, 80)

                @block.vector
                def _(v):
                    link = Chain(v, s_ch)
                    v.wait_ge(s_in, 80)
                    for h in range(HEADS):
                        sl = hh[:, :, h * OC:(h + 1) * OC]
                        ins = v.tensor_tensor(sl, sl, col(wgt[:, h, :], P, NB, OC), ALU.mult)
                    link(ins)
                    link(v.tensor_tensor(hh[:, :, :], hh[:, :, :], row(bias_b[:, :], P, NB, D), ALU.add))
                    v.tensor_tensor(x2[:, :, :], x2[:, :, :], hh[:, :, :], ALU.add).then_inc(s_x2, 1)
                    v.wait_ge(s_x2, 1)

            s_qm, s_pm, s_p3 = sem("q_moved"), sem("p_moved"), sem("p_chain")
            s_qs = [sem(f"q_stored{k}") for k in range(2)]
            s_xs = sem("x2_stored")
            block = ctx.enter_context(nc.Block())

            @block.sync
            def _(sp):
                sp.dma_start(x2_d.rearrange("(b p) d -> p b d", p=P), x2[:, :, :]).then_inc(s_xs, 16)
                sp.wait_ge(s_xs, 16)

            w1f = w1[:, :, :].rearrange("p s f -> p (s f)")

            def ready(eng):
                eng.wait_ge(s_x2, 1)

            def evacuate(act, b, par, ps, moved):
                if not first(b, 2):
                    act.wait_ge(s_qs[par], (b - par) * 8)
                    act.wait_ge(s_p3, (b - 1) * 5)
                act.activation(qrow[:, par, :], ps[:, HID:2 * HID], ACT.Copy).then_inc(s_qm, 1)
                act.activation(prow[:, par, :], ps[:, 0:HID], ACT.Copy).then_inc(moved, 1)
                act.wait_ge(s_qm, b + 1)
                act.dma_start(q_d.rearrange("(b p) d -> b p d", p=P)[bass.ds(b, 1), :, :].rearrange("o p d -> (o p) d"),
                              qrow[:, par, :]).then_inc(s_qs[par], 16)

            def split(v, b, par, moved):
                p = prow[:, par, :]
                part3 = lambda k: pn[:, bass.ds(b, 1), k, :].rearrange("p o f -> p (o f)")
                v.wait_ge(moved, b + 1)
                v.tensor_tensor(p, p, b1_b[:, :], ALU.add).then_inc(s_p3, 1)
                for k in range(2):
                    v.wait_ge(s_p3, b * 5 + (2 * k + 1))
                    v.tensor_copy(part3(k), p).then_inc(s_p3, 1)
                    v.wait_ge(s_p3, b * 5 + (2 * k + 2))
                    v.tensor_tensor(p, p, part3(k), ALU.subtract).then_inc((s_p3, s_pm)[k], 1)
                v.wait_ge(s_pm, b + 1)
                v.tensor_copy(part3(2), p).then_inc(s_p3, 1)

            normed_product(block, ctx, "l1_", x2, w1f, 2 * HID, ready, evacuate, split)

            @block.scalar
            def _(act):
                act.wait_ge(s_qs[0], 16 * (NB - NB // 2))
                act.wait_ge(s_qs[1], 16 * (NB // 2))

        agg = sb("agg", [P, NB, HID], F32)
        with ExitStack() as ctx:
            PG, LAG = G // 2, 2
            w1c = sb("w1c", [ED, HID], F32, ctx)
            rec = sb("g_rec", [P, 2, G, REC], F32, ctx)
            lrow = sb("g_lrow", [P, 2, GE], BF16, ctx)
            ohT = sb("g_ohT", [P, 2, G // 2, P, 2], BF16, ctx)
            oh = sb("g_oh", [P, 2, G, P], F32, ctx)
            idx_f = sb("g_idx_f", [P, G], F32, ctx)
            idx = sb("g_idx", [P, 2, G], I32, ctx)
            qg = sb("g_q", [P, 2, G, HID], F32, ctx)
            eaT = sb("g_eaT", [ED, 2, G, P], F32, ctx)
            hid = sb("g_hid", [P, G, HID], F32, ctx)
            tp = [pb(f"g_tp{k}", ctx) for k in range(2)]
            hp = [pb(f"g_hp{k}", ctx) for k in range(4)]
            ap = [pb(f"g_ap{k}", ctx) for k in range(2)]
            s_w = sem("w1c_loaded")
            s_ld = [sem(f"g_loaded{k}") for k in range(2)]
            s_q = [sem(f"g_gathered{k}") for k in range(2)]
            s_if, s_idx, s_oh, s_az = sem("g_idx_f"), sem("g_idx_ready"), sem("g_onehot_ready"), sem("agg_zeroed")
            s_tp, s_eaT, s_hp, s_pre = sem("g_turned"), sem("g_eaT_ready"), sem("g_product"), sem("g_pre_ready")
            s_hid, s_ap, s_agg, s_go2 = sem("g_hidden_ready"), sem("g_pair_summed"), sem("g_added"), sem("gather_begun")
            s_tb, s_lb = sem("g_turn_begun"), sem("g_load_begun")
            block = ctx.enter_context(nc.Block())

            @block.sync
            def _(sp):
                sp.dma_start(w1c[:, :], W1[2 * D:2 * D + ED, :]).then_inc(s_w, 16)

                def load(g, par):
                    if not first(g, 2):
                        sp.wait_ge(s_oh, g - 1)
                        sp.sem_inc(s_lb, 1)
                        sp.wait_ge(s_tp, (g - 1) * 2)
                    one = bass.ds(g, 1)
                    sp.dma_start(rec[:, par, :, :].rearrange("p (u k) f -> p u (k f)", k=2),
                                 rec_d.rearrange("(g u p k) f -> g p u (k f)", p=P, k=2, u=PG)[one, :, :, :]
                                 .rearrange("o p u f -> (o p) u f")).then_inc(s_ld[par], 16)
                    sp.dma_start(lrow[:, par, :], low_row_d.rearrange("(g e) -> g e", e=GE)[one, :]
                                 .to_broadcast([P, GE])).then_inc(s_ld[par], 16)

                pairs(sp, load, NGS)

            @block.gpsimd
            def _(pool):
                def gather(g, par):
                    pool.wait_ge(s_idx, g + 1)
                    if not first(g, 2):
                        pool.wait_ge(s_hid, (g - 1) * G)
                    pool.sem_inc(s_go2, 1)
                    for j in range(G):
                        pool.indirect_dma_start(qg[:, par, j, :], None, q_d,
                                                bass.IndirectOffsetOnAxis(ap=idx[:, par, j:j + 1], axis=0)).then_inc(s_q[par], 16)

                pairs(pool, gather, NGS)

            @block.vector
            def _(v):
                v.memset(agg[:, :, :], 0.0).then_inc(s_az, 1)
                v.wait_ge(s_az, 1)

                def prepare(g, par):
                    v.wait_ge(s_ld[par], (g - par) * 16 + 32)
                    if not first(g):
                        v.wait_ge(s_idx, g)
                    v.tensor_scalar(idx_f[:, :], rec[:, par, :, F_DST], 0.0, None, ALU.max).then_inc(s_if, 1)
                    v.wait_ge(s_if, g + 1)
                    if not first(g, 2):
                        v.wait_ge(s_q[par], (g - par) * (8 * G))
                    v.tensor_copy(idx[:, par, :], idx_f[:, :]).then_inc(s_idx, 1)
                    if not first(g, 2):
                        v.wait_ge(s_hp, (g - 1) * G)
                        v.wait_ge(s_ap, (g - 1) * PG)
                    v.tensor_scalar(ohT[:, par, :, :, :].rearrange("p u q k -> p (u q k)"), lrow[:, par, :], part[:, 0:1], None, ALU.is_equal)
                    for j in range(G):
                        ins = v.tensor_scalar(oh[:, par, j, :], iota[:, :], rec[:, par, j, F_LOW:F_LOW + 1], None, ALU.is_equal)
                    ins.then_inc(s_oh, 1)

                def add(g, par, u):
                    if u == 0:
                        v.wait_ge(s_q[par], (g - par) * (8 * G) + 16 * G)
                    for j in (2 * u, 2 * u + 1):
                        v.wait_ge(s_hp, g * G + (j + 1))
                        v.tensor_tensor(qg[:, par, j, :], hp[j % 4][:, 0:HID], qg[:, par, j, :], ALU.add).then_inc(s_pre, 1)

                def collect(g, u):
                    b = v.value_load(blk[0:1, bass.ds(g * PG + u, 1)], min_val=0, max_val=NB - 1)
                    v.wait_ge(s_ap, g * PG + (u + 1))
                    if not (first(g) and u == 0):
                        v.wait_ge(s_agg, g * PG + u)
                    to = agg[:, bass.ds(b, 1), :].rearrange("p o f -> p (o f)")
                    v.tensor_tensor(to, to, ap[u % 2][:, 0:HID], ALU.add).then_inc(s_agg, 1)

                def group(g, par, last=False):
                    for u in range(PG):
                        add(g, par, u)
                        if u >= LAG + 1:
                            collect(g, u - LAG - 1)
                        elif not first(g):
                            collect(g - 1, PG + u - LAG - 1)
                        if u == 1 and not last:
                            prepare(g + 1, 1 - par)

                prepare(0, 0)
                group(0, 0)
                group(1, 1)
                with v.Fori(1, NGS // 2 - 1) as i:
                    group(i * 2, 0)
                    group(i * 2 + 1, 1)
                group(NGS - 2, 0)
                group(NGS - 1, 1, last=True)
                for u in range(PG - LAG - 1, PG):
                    collect(NGS - 1, u)

            @block.scalar
            def _(act):
                def turned(g, par):
                    for k in range(2):
                        act.wait_ge(s_tp, g * 2 + (k + 1))
                        if k == 0 and not first(g, 2):
                            act.wait_ge(s_hp, (g - 1) * G)
                        act.activation(eaT[:, par, 4 * k:4 * k + 4, :].rearrange("p j e -> p (j e)"),
                                       tp[k][0:ED, :], ACT.Copy).then_inc(s_eaT, 1)

                def group(g, par, last=False):
                    for j in range(G):
                        if j == 4 and not last:
                            turned(g + 1, 1 - par)
                        if not first(g):
                            act.wait_ge(s_ap, g * PG - PG + (j // 2 + 1))
                        act.wait_ge(s_pre, g * G + (j + 1))
                        act.activation(hid[:, j, :], qg[:, par, j, :], ACT.Relu).then_inc(s_hid, 1)

                turned(0, 0)
                group(0, 0)
                group(1, 1)
                with act.Fori(1, NGS // 2 - 1) as i:
                    group(i * 2, 0)
                    group(i * 2 + 1, 1)
                group(NGS - 2, 0)
                group(NGS - 1, 1, last=True)

            @block.tensor
            def _(pe):
                def turn(g, par):
                    pe.wait_ge(s_ld[par], (g - par) * 16 + 32)
                    for k in range(2):
                        if not first(g):
                            pe.wait_ge(s_eaT, g * 2 - 2 + (k + 1))
                        pe.sem_inc(s_tb, 1)
                        for j in range(4):
                            mm = pe.transpose(tp[k][0:ED, j * P:(j + 1) * P], rec[:, par, 4 * k + j, 0:ED], ident[:, :])
                        mm.then_inc(s_tp, 1)

                def block_of(g, u):
                    return pe.value_load(blk[0:1, bass.ds(g * PG + u, 1)], min_val=0, max_val=NB - 1)

                def hidden(g, par, u, b):
                    if u == 0:
                        pe.wait_ge(s_oh, g + 1)
                    if u % 2 == 0:
                        pe.wait_ge(s_eaT, g * 2 + (u // 2 + 1))
                    for k in range(2):
                        j = 2 * u + k
                        if not (first(g) and j < 4):
                            pe.wait_ge(s_pre, g * G + (j - 3) if j >= 3 else g * G - (3 - j))
                        to = hp[j % 4][:, 0:HID]
                        pe.matmul(to, eaT[:, par, j, :], w1c[:, :], start=True, stop=False)
                        for s in range(3):
                            mm = pe.matmul(to, ohT[:, par, u, :, k],
                                           pn[:, bass.ds(b, 1), s, :].rearrange("p o f -> p (o f)"),
                                           start=False, stop=(s == 2))
                        mm.then_inc(s_hp, 1)

                def summed(g, par, u):
                    if not (first(g) and u < 2):
                        pe.wait_ge(s_agg, g * PG + (u - 1) if u >= 1 else g * PG - 1)
                    for k in range(2):
                        j = 2 * u + k
                        pe.wait_ge(s_hid, g * G + (j + 1))
                        mm = pe.matmul(ap[u % 2][:, 0:HID], oh[:, par, j, :], hid[:, j, :], start=(k == 0), stop=(k == 1))
                    mm.then_inc(s_ap, 1)

                def group(g, par, last=False):
                    b = block_of(g, 0)
                    for u in range(PG):
                        hidden(g, par, u, b)
                        if u < PG - 1:
                            b = block_of(g, u + 1)
                        if u >= LAG:
                            summed(g, par, u - LAG)
                        elif not first(g):
                            summed(g - 1, 1 - par, PG + u - LAG)
                        if u == 2 and not last:
                            turn(g + 1, 1 - par)

                pe.wait_ge(s_w, 16)
                turn(0, 0)
                group(0, 0)
                group(1, 1)
                with pe.Fori(1, NGS // 2 - 1) as i:
                    group(i * 2, 0)
                    group(i * 2 + 1, 1)
                group(NGS - 2, 0)
                group(NGS - 1, 1, last=True)
                for u in range(PG - LAG, PG):
                    summed(NGS - 1, 1, u)

        with ExitStack() as ctx:
            x2 = sb("x2_out", [P, NB, D], F32, ctx)
            w2 = sb("w2", [P, 2, D], F32, ctx)
            b2_b = sb("b2_b", [P, D], F32, ctx)
            ab = sb("ab", [P, 2, HID], F32, ctx)
            aT = sb("aT", [P, 2, 2, P], F32, ctx)
            tp = [pb(f"o_tp{k}", ctx) for k in range(2)]
            op = [pb(f"o_op{k}", ctx) for k in range(2)]
            s_in, s_b, s_tp, s_aT, s_op = sem("o_inputs"), sem("o_staged"), sem("o_turned"), sem("o_aT_ready"), sem("o_product")
            s_d, s_x, s_o = sem("o_bias_added"), sem("o_row_ready"), sem("o_stored")
            block = ctx.enter_context(nc.Block())
            full_b = NODES // P

            @block.sync
            def _(sp):
                sp.dma_start(x2[:, :, :], x2_d.rearrange("(b p) d -> p b d", p=P)).then_inc(s_in, 16)
                sp.dma_start(w2[:, :, :], W2.rearrange("(s p) d -> p s d", p=P)).then_inc(s_in, 16)
                sp.dma_start(b2_b[:, :], b2.rearrange("(o f) -> o f", o=1).to_broadcast([P, D])).then_inc(s_in, 16)
                sp.wait_ge(s_x, NB)
                sp.dma_start(out[0:full_b * P, :].rearrange("(b p) d -> p b d", p=P), x2[:, 0:full_b, :]).then_inc(s_o, 16)
                sp.dma_start(out[full_b * P:NODES, :], x2[0:NODES - full_b * P, full_b, :]).then_inc(s_o, 16)
                sp.wait_ge(s_o, 32)

            @block.vector
            def _(v):
                v.wait_ge(s_in, 48)

                def stage(b, par):
                    freed(v, s_tp, b)
                    v.tensor_copy(ab[:, par, :], agg[:, bass.ds(b, 1), :].rearrange("p o f -> p (o f)")).then_inc(s_b, 1)
                    xb = x2[:, bass.ds(b, 1), :].rearrange("p o d -> p (o d)")
                    v.scalar_tensor_tensor(out=xb, in0=b2_b[:, :], scalar=deg[:, bass.ds(b, 1)], in1=xb,
                                           op0=ALU.mult, op1=ALU.add).then_inc(s_d, 1)
                    v.wait_ge(s_op, b + 1)
                    v.wait_ge(s_d, b + 1)
                    v.tensor_tensor(xb, xb, op[par][:, 0:D], ALU.add).then_inc(s_x, 1)

                pairs(v, stage, NB)

            @block.scalar
            def _(act):
                def turned(b, par):
                    act.wait_ge(s_tp, b + 1)
                    freed(act, s_op, b)
                    act.activation(aT[:, par, :, :].rearrange("p s n -> p (s n)"), tp[par][:, 0:2 * P], ACT.Copy).then_inc(s_aT, 1)

                pairs(act, turned, NB)

            @block.tensor
            def _(pe):
                pe.wait_ge(s_in, 48)

                def product(b, par):
                    pe.wait_ge(s_b, b + 1)
                    freed(pe, s_aT, b)
                    for s in range(2):
                        mm = pe.transpose(tp[par][:, s * P:(s + 1) * P], ab[:, par, s * P:(s + 1) * P], ident[:, :])
                    mm.then_inc(s_tp, 1)
                    pe.wait_ge(s_aT, b + 1)
                    freed(pe, s_x, b)
                    for s in range(2):
                        mm = pe.matmul(op[par][:, 0:D], aT[:, par, s, :], w2[:, s, :], start=(s == 0), stop=(s == 1))
                    mm.then_inc(s_op, 1)

                pairs(pe, product, NB)


def kernel(x, src, dst, edge_attr_64, L0_gnn_W, L0_gnn_att, L0_gnn_bias, L1_gnn_W1, L1_gnn_b1, L1_gnn_W2, L1_gnn_b2):
    import numpy as np
    import concourse.bacc as bacc
    from concourse.bass_utils import run_bass_kernel_spmd

    def padded(a, n, fill):
        a = np.asarray(a)
        return np.concatenate([a, np.full((n - a.shape[0],) + a.shape[1:], fill, a.dtype)])

    arrays = {
        "x": padded(x, NODES_P, 0), "src": padded(src, EDGES_P, NODES_P - 1), "dst": padded(dst, EDGES_P, NODES_P - 1),
        "ea": padded(edge_attr_64, EDGES_P, 0), "W": L0_gnn_W, "att": L0_gnn_att, "bias": L0_gnn_bias,
        "W1": L1_gnn_W1, "b1": L1_gnn_b1, "W2": L1_gnn_W2, "b2": L1_gnn_b2,
    }
    arrays = {f"in_{k}": np.ascontiguousarray(a) for k, a in arrays.items()}
    nc = bacc.Bacc("TRN2", target_bir_lowering=False, num_devices=1)
    args = [nc.dram_tensor(n, a.shape, mybir.dt.from_np(a.dtype), kind="ExternalInput").ap() for n, a in arrays.items()]
    out = nc.dram_tensor("out", (NODES, D), F32, kind="ExternalOutput").ap()
    build(nc, *args, out)
    r = run_bass_kernel_spmd(nc, [arrays], core_ids=[0])
    return r.results[0]["out"]
```
